# Optimizing a Trainium2 kernel written in Bass

```python
import numpy as np
import jax
import jax.numpy as jnp

def _softmax(x, axis=-1):
    return jax.nn.softmax(x, axis=axis)

def _gelu(x):
    return jax.nn.gelu(x, approximate=True)

def _silu(x):
    return jax.nn.silu(x)

def _sigmoid(x):
    return jax.nn.sigmoid(x)

def _layernorm(x, axis=-1, eps=1e-05):
    m = jnp.mean(x, axis=axis, keepdims=True)
    v = jnp.var(x, axis=axis, keepdims=True)
    return (x - m) / jnp.sqrt(v + eps)

def _scatter_add(tgt, idx, src, axis=0):
    return tgt.at[idx].add(src)

def _segment_sum(src, seg, n):
    return jax.ops.segment_sum(src, seg, n)
kernel_name = 'mk_adj_preln_d2_adj_r2_040949'

def setup_inputs(seed: int=0):
    np.random.seed(seed)
    _w = jnp.asarray

    def _rec_inputs():
        import jax
        import jax.numpy as jnp
        _gk = jax.random.key(seed)
        x = -0.000929 + 1 * jax.random.normal(jax.random.fold_in(_gk, 1), (8, 1024, 256), jnp.float32)
        _a = jax.random.bernoulli(jax.random.fold_in(_gk, 2), 0.015625, (1024, 1024))
        _a = jnp.logical_or(_a, jnp.swapaxes(_a, -1, -2))
        _a = jnp.logical_or(_a, jnp.eye(1024, dtype=bool))
        adj = _a.astype(jnp.int32)
        return (x, adj)
    x, adj = _rec_inputs()

    def _L0_gnn_setup():
        import jax, jax.numpy as jnp
        import numpy as np
        B, K, DIN, DOUT = (32, 64, 256, 256)
        key = jax.random.key(seed)
        k1, k2, k3, k4 = jax.random.split(key, 4)
        x = jax.random.normal(k1, (B, K, DIN), dtype=jnp.float32)
        adj = jax.random.randint(k2, (K, K), 0, 2, dtype=jnp.int32)
        W = jax.random.normal(k3, (DOUT, 2 * DIN), dtype=jnp.float32) * 0.02
        b = jax.random.normal(k4, (DOUT,), dtype=jnp.float32) * 0.02
        return {'x': x, 'adj': adj, 'W': W, 'b': b}
    _L0_gnn_all = _L0_gnn_setup()
    _L0_gnn_in = {k: v for k, v in _L0_gnn_all.items() if k in ('W', 'b')}
    del _L0_gnn_all

    def _L1_gnn_setup():
        import jax, jax.numpy as jnp
        import numpy as np
        B, N, F, F1 = (512, 75, 256, 128)
        NEG = -1000000000.0
        ALPHA = 0.2
        key = jax.random.key(seed)
        k1, k2, k3, k4 = jax.random.split(key, 4)
        X = jax.random.normal(k1, (B, N, F), dtype=jnp.float32)
        A = jax.random.randint(k2, (N, N), 0, 2, dtype=jnp.int32)
        W = jax.random.normal(k3, (F, F1), dtype=jnp.float32) * (1.0 / np.sqrt(F))
        a = jax.random.normal(k4, (2, F1, 1), dtype=jnp.float32) * (1.0 / np.sqrt(F1))
        return {'X': X, 'A': A, 'W': W, 'a': a}
    _L1_gnn_all = _L1_gnn_setup()
    _L1_gnn_in = {k: v for k, v in _L1_gnn_all.items() if k in ('W', 'a')}
    del _L1_gnn_all
    return {'x': x, 'adj': adj, 'L0_gnn_W': _L0_gnn_in['W'], 'L0_gnn_b': _L0_gnn_in['b'], 'L1_gnn_W': _L1_gnn_in['W'], 'L1_gnn_a': _L1_gnn_in['a']}

def reference(x, adj, L0_gnn_W, L0_gnn_b, L1_gnn_W, L1_gnn_a):
    import jax
    import jax.numpy as jnp

    def _L0_gnn_ref(x, adj, W, b):
        import jax, jax.numpy as jnp
        import numpy as np
        B, K, DIN, DOUT = (32, 64, 256, 256)
        Din = x.shape[-1]
        Wi, Wj = (W[:, :Din], W[:, Din:])
        mi = jnp.einsum('bkd,od->bko', x, Wi)
        mj = jnp.einsum('bkd,od->bko', x, Wj)
        a = adj.astype(x.dtype)
        deg = a.sum(axis=1)
        out = deg[None, :, None] * (mi + b) + jnp.einsum('ij,bjo->bio', a, mj)
        return out

    def _L1_gnn_ref(X, A, W, a):
        import jax, jax.numpy as jnp
        import numpy as np
        B, N, F, F1 = (512, 75, 256, 128)
        NEG = -1000000000.0
        ALPHA = 0.2
        h = jnp.einsum('bnf,fo->bno', X, W)
        att_self = jnp.einsum('bno,od->bnd', h, a[0])
        att_neigh = jnp.einsum('bno,od->bnd', h, a[1])
        e = att_self + jnp.swapaxes(att_neigh, 1, 2)
        e = jax.nn.leaky_relu(e, ALPHA)
        adj = A.astype(h.dtype)
        e = e + NEG * (1.0 - adj)[None, :, :]
        alpha = jax.nn.softmax(e, axis=-1)
        out = jnp.einsum('bij,bjo->bio', alpha, h)
        return jnp.concatenate([out, h], axis=-1)
    h = jnp.maximum(_layernorm(x, axis=-1), 0.0)
    x = x + _L0_gnn_ref(h, adj, L0_gnn_W, L0_gnn_b)
    h = jnp.maximum(_layernorm(x, axis=-1), 0.0)
    x = x + _L1_gnn_ref(h, adj, L1_gnn_W, L1_gnn_a)
    return x

_drawn_inputs = setup_inputs


def setup_inputs(seed=0):
    import zlib

    import numpy as np

    out = dict(_drawn_inputs(seed))
    spreads = {}
    factors = {'L1_gnn_a': 8.0}
    for name, (base, spread) in spreads.items():
        noise = np.random.default_rng([zlib.crc32(name.encode()), seed]).standard_normal(out[name].shape)
        drawn = base * np.exp(spread * noise) if base else spread * noise
        out[name] = jnp.asarray(drawn.astype(out[name].dtype))
    for name, factor in factors.items():
        out[name] = (out[name] * factor).astype(out[name].dtype)
    return out
```

```python
from contextlib import ExitStack

import concourse.bass as bass
from concourse import mybir

F32 = mybir.dt.float32
F32R = mybir.dt.float32r
I32 = mybir.dt.int32
ALU = mybir.AluOpType
ACT = mybir.ActivationFunctionType

P = 128
NEG = -1.0e9
SLOPE = 0.2
EPS = 1e-5
FAR = 3.0e38

ITERATION = [
    ("S1", 0), ("SM", 1), ("TP", 0), ("OBprev", 1), ("T1", 0), ("S1", 1), ("L0", 0), ("L0", 1),
    ("SM", 2), ("TP", 1), ("L0", 2), ("L0", 3), ("T1", 1),
    ("SM", 3), ("TP", 2), ("L0", 4), ("L0", 5), ("L0", 6),
    ("SM", 4), ("TP", 3), ("L0", 7), ("AG", 0),
    ("SM", 5), ("AT", 0), ("TP", 4), ("AG", 1), ("OB", 0),
    ("SM", 6), ("TP", 5), ("S2", 0), ("AG", 2), ("T2", 0),
    ("SM", 7), ("TP", 6), ("AG", 3), ("HH", 0), ("S2", 1), ("NB", 0),
    ("TP", 7), ("T2", 1), ("HH", 1), ("NB", 1), ("TH", 0), ("TH", 1), ("AT", 1),
    ("NEXTSM", 0), ("HS", 0), ("HS", 1),
]
LAST = [
    ("SM", 1), ("TP", 0), ("OBprev", 1), ("SM", 2), ("TP", 1), ("SM", 3), ("TP", 2), ("SM", 4), ("TP", 3),
    ("SM", 5), ("AT", 0), ("TP", 4), ("OB", 0), ("SM", 6), ("TP", 5), ("SM", 7), ("TP", 6), ("TP", 7),
    ("AT", 1), ("OB", 1),
]
SHARED = (1, 3, 5, 7)
STAGE_C = ("SM", "TP", "AT", "OB")
STAGE_A = [(name, i) for name, i in ITERATION if name not in STAGE_C + ("OBprev", "NEXTSM")]

PER_BATCH = {"T1": 4, "L0": 8, "AG": 4, "T2": 4, "HH": 2, "NB": 2, "TH": 2}
A_GROUPS = [(name, i, k) for name, i in STAGE_A if name in PER_BATCH for k in range(2 if name in ("T1", "T2") else 1)]
A_BANKS = 3
A_SLOTS = -(-len(A_GROUPS) // A_BANKS) * A_BANKS


def ring_before(step, i, k):
    at = A_GROUPS.index((step, i, k)) - A_BANKS
    earlier = at < 0
    at %= A_SLOTS
    while at >= len(A_GROUPS):
        at -= A_BANKS
    return A_GROUPS[at], earlier


def ordinal(step, i, k):
    return 1 + (2 * i + k if step in ("T1", "T2") else i)


def build(nc, x, adj, adj_t, w_cat_t, bias, w_att, a_self, a_neigh, identity, out):
    B, _, D = x.shape
    T = 8
    N = P * T
    H = D // 2
    K = D // P
    assert D == 2 * P and w_cat_t.shape == (D, 2 * D) and w_att.shape == (D, H)

    x_rows = x.rearrange("b (p t) d -> b p t d", p=P)
    out_rows = out.rearrange("b (p t) d -> b p t d", p=P)

    ctx = ExitStack()
    with ctx:
        def sb(name, shape, dt=F32):
            return ctx.enter_context(nc.sbuf_tensor(name, shape, dt))

        def sem(name):
            return ctx.enter_context(nc.semaphore(name))

        adjT = sb("adjT", [P, T, N], F32R)
        mask = sb("mask", [P, T, N])
        wl_hi = sb("wl_hi", [P, K, 2 * D], F32R)
        wl_lo = sb("wl_lo", [P, K, 2 * D], F32R)
        wa_hi = sb("wa_hi", [P, K, H], F32R)
        wa_lo = sb("wa_lo", [P, K, H], F32R)
        wa_raw = sb("wa_raw", [P, K, H])
        a0_bc = sb("a0_bc", [P, H])
        a1_col = sb("a1_col", [P, 1])
        ident = sb("ident", [P, P])
        degb = sb("degb", [P, T, D])
        deg = sb("deg", [P, T])
        xs = [sb(f"x{i}", [P, T, D]) for i in range(2)]
        xn = sb("xn", [P, 2, 4, D])
        stats = sb("stats", [P, 2, 2, 4, 6])
        moments = sb("moments", [P, 2, 4, 2])
        neg_mean = sb("neg_mean", [P, 2, 2, 4])
        var_eps = sb("var_eps", [P, 2, 2, 4])
        rstd = sb("rstd", [P, 2, 2, 4])
        minus_half = sb("minus_half", [P, 4])
        hT_hi = sb("hT_hi", [P, K, N], F32R)
        hT_lo = sb("hT_lo", [P, K, N], F32R)
        mj_hi = sb("mj_hi", [P, T, D], F32R)
        mj_lo = sb("mj_lo", [P, T, D], F32R)
        hhT = sb("hhT", [P, 2, N // 2])
        hh_hi = sb("hh_hi", [P, T, H], F32R)
        hh_lo = sb("hh_lo", [P, T, H], F32R)
        n_bc = sb("n_bc", [P, N])
        n_slope = sb("n_slope", [P, N])
        s_rest = sb("s_rest", [P, T])
        neg_max = sb("neg_max", [P, T])
        den = sb("den", [P, T])
        rden = sb("rden", [P, T])
        p_row = sb("p_row", [P, 2, N])
        n_mask = sb("n_mask", [P, N])
        pT_hi = sb("pT_hi", [P, T, N // 2], F32R)
        pT_lo = sb("pT_lo", [P, T, N // 2], F32R)
        oT = sb("oT", [P, N // 2])

        ring = [ctx.enter_context(nc.psum_tensor(f"ring{i}", [P, 512], F32)) for i in range(A_BANKS)]
        p_bank = [ctx.enter_context(nc.psum_tensor(f"p_bank{i}", [P, 512], F32)) for i in range(4)]
        o_bank = ctx.enter_context(nc.psum_tensor("o_bank", [P, 512], F32))

        x_loaded = [[sem(f"x_loaded{i}{c}") for c in range(2)] for i in range(2)]
        adjt_loaded = [sem(f"adjt_loaded{t}") for t in range(2)]
        adj_loaded = [sem(f"adj_loaded{t}") for t in range(2)]
        weights_loaded = sem("weights_loaded")
        small_loaded = sem("small_loaded")
        stored = sem("stored")
        adjt_ready = sem("adjt_ready")
        mask_ready = sem("mask_ready")
        deg_ready = sem("deg_ready")
        degb_ready = sem("degb_ready")
        whi_ready = sem("whi_ready")
        w_ready = sem("w_ready")
        half_ready = sem("half_ready")
        done = {s: sem(f"{s}_done") for s in PER_BATCH}
        tp_done = sem("tp_done")
        att_done = sem("att_done")
        ob_done = sem("ob_done")
        t_lo = {s: sem(f"{s}_lo") for s in ("T1", "T2")}
        t_hi = {s: sem(f"{s}_hi") for s in ("T1", "T2")}
        l0_read = sem("l0_read")
        x1_ready = sem("x1_ready")
        hht_ready = sem("hht_ready")
        nb_ready = sem("nb_ready")
        hh_ready = sem("hh_ready")
        ring_read = {"T1": t_lo["T1"], "T2": t_lo["T2"], "L0": l0_read, "AG": x1_ready, "HH": hht_ready,
                     "NB": nb_ready, "TH": hh_ready}
        dve_passed = sem("dve_passed")
        pool_passed = sem("pool_passed")
        bn_done = {s: sem(f"{s}_bn") for s in ("S1", "S2")}
        moments_ready = {s: sem(f"{s}_moments") for s in ("S1", "S2")}
        pool_step = sem("pool_step")
        xn_ready = {s: sem(f"{s}_xn") for s in ("S1", "S2")}
        xb_ready = sem("xb_ready")
        mjhi_ready = sem("mjhi_ready")
        s_ready = sem("s_ready")
        xh_ready = sem("xh_ready")
        hhhi_ready = sem("hhhi_ready")
        leaky_ready = sem("leaky_ready")
        relu_ready = sem("relu_ready")
        nmask_ready = sem("nmask_ready")
        e_ready = sem("e_ready")
        p_ready = sem("p_ready")
        phi_ready = sem("phi_ready")
        plo_ready = sem("plo_ready")
        oT_ready = sem("oT_ready")
        rden_ready = sem("rden_ready")
        out_ready = sem("out_ready")

        block = ctx.enter_context(nc.Block())

        def after(eng, s, n, per, b):
            if isinstance(b, int) and b * per + n <= 0:
                return
            eng.wait_ge(s, b * per + n)

        def run(eng, step, last_step=None):
            for name, i in STAGE_A:
                step(name, i, 0, 0, 0)
            step("SM", 0, 0, 0, 0)

            def iteration(order, b, half, nxt, nxt_half, odd):
                for name, i in order:
                    if name == "OBprev":
                        if not isinstance(b, int) or b > 0:
                            step("OB", i, b - 1, 1 - odd, half)
                    elif name == "NEXTSM":
                        step("SM", i, nxt, 1 - odd, nxt_half)
                    elif name in STAGE_C:
                        step(name, i, b, odd, half)
                    else:
                        step(name, i, nxt, 1 - odd, nxt_half)

            iteration(ITERATION, 0, 0, 1, 0, 0)
            with eng.Fori(0, (B - 2) // 2) as t:
                iteration(ITERATION, t * 2 + 1, t, t * 2 + 2, t + 1, 1)
                iteration(ITERATION, t * 2 + 2, t + 1, t * 2 + 3, t + 1, 0)
            iteration(LAST, B - 1, (B - 1) // 2, None, None, 1)

        @block.sync
        def _(sp):
            def load_x(b, parity, c):
                sp.dma_start(xs[parity][:, 4 * c:4 * c + 4, :],
                             x_rows[b, :, 4 * c:4 * c + 4, :]).then_inc(x_loaded[parity][c], 16)

            def store_out(b, parity, c):
                sp.wait_ge(out_ready, b * 2 + (c + 1))
                sp.dma_start(out_rows[b, :, 4 * c:4 * c + 4, :],
                             xs[parity][:, 4 * c:4 * c + 4, :]).then_inc(stored, 16)
                sp.wait_ge(stored, b * 32 + (16 * c + 16))

            load_x(0, 0, 0)
            sp.dma_start(p_row[:, :, 0:2 * D], w_cat_t.rearrange("(k p) o -> p k o", p=P)).then_inc(weights_loaded, 16)
            load_x(0, 0, 1)
            sp.dma_start(mask[:, 0:4, :].bitcast(I32), adj_t[:, 0:4, :]).then_inc(adjt_loaded[0], 16)
            sp.dma_start(mask[:, 4:8, :].bitcast(I32), adj_t[:, 4:8, :]).then_inc(adjt_loaded[1], 16)
            load_x(1, 1, 0)
            load_x(1, 1, 1)
            for h in range(2):
                sp.wait_ge(adjt_ready, 4 * h + 4)
                sp.dma_start(mask[:, 4 * h:4 * h + 4, :].bitcast(I32),
                             adj[:, 4 * h:4 * h + 4, :]).then_inc(adj_loaded[h], 16)
            for c in range(2):
                store_out(0, 0, c)
                load_x(2, 0, c)
            with sp.Fori(0, (B - 4) // 2) as t:
                for c in range(2):
                    store_out(t * 2 + 1, 1, c)
                    load_x(t * 2 + 3, 1, c)
                for c in range(2):
                    store_out(t * 2 + 2, 0, c)
                    load_x(t * 2 + 4, 0, c)
            for c in range(2):
                store_out(B - 3, 1, c)
                load_x(B - 1, 1, c)
            for b in (B - 2, B - 1):
                for c in range(2):
                    store_out(b, b % 2, c)

        @block.gpsimd
        def _(pool):
            pool_steps = [0]
            pool.memset(minus_half[:], -0.5).then_inc(half_ready, 1)
            pool.wait_ge(half_ready, 1)

            def step(name, i, b, parity, half):
                if name in ("S1", "S2"):
                    which = int(name == "S2")
                    xt = xs[parity]
                    pool.wait_ge(moments_ready[name], b * 2 + (i + 1))
                    after(pool, xn_ready[name], i + 1 - 2, 2, b)
                    pool.sem_inc(pool_passed)
                    pool.tensor_scalar(var_eps[:, which, i, :], moments[:, i, :, 1], EPS, 1.0, ALU.add,
                                       ALU.mult).then_inc(pool_step, 1)
                    pool.tensor_scalar(neg_mean[:, which, i, :], moments[:, i, :, 0], -1.0, 0.0, ALU.mult,
                                       ALU.add).then_inc(pool_step, 1)
                    at = 3 * (2 * which + i)
                    pool.wait_ge(pool_step, b * 12 + (at + 2))
                    pool.tensor_tensor(rstd[:, which, i, :], var_eps[:, which, i, :], minus_half[:],
                                       ALU.pow).then_inc(pool_step, 1)
                    pool.wait_ge(pool_step, b * 12 + (at + 3))
                    if which:
                        pool.wait_ge(done["T1"], b * 4 + (2 * i + 2))
                    else:
                        after(pool, done["T2"], 2 * i + 2 - 4, 4, b)
                    pool.sem_inc(pool_passed)
                    for q in range(4):
                        ins = pool.tensor_scalar(xn[:, i, q, :], xt[:, 4 * i + q, :], neg_mean[:, which, i, q:q + 1],
                                                 rstd[:, which, i, q:q + 1], ALU.add, ALU.mult)
                    ins.then_inc(xn_ready[name], 1)
                    if not which:
                        pool.wait_ge(xn_ready[name], b * 2 + (i + 1))
                        if isinstance(b, int) and b == 0:
                            pool.wait_ge(degb_ready, 1)
                        pool.tensor_tensor(xt[:, 4 * i:4 * i + 4, :], xt[:, 4 * i:4 * i + 4, :],
                                           degb[:, 4 * i:4 * i + 4, :], ALU.add).then_inc(xb_ready, 1)
                elif name == "SM" and i in SHARED:
                    at = SHARED.index(i)
                    pool.wait_ge(nb_ready, b * 2 + 2)
                    if at:
                        pool.wait_ge(e_ready, b * 8 + (SHARED[at - 1] + 1))
                    else:
                        after(pool, e_ready, SHARED[-1] + 1 - 8, 8, b)
                    if isinstance(b, int) and b == 0:
                        pool.wait_ge(mask_ready, 2)
                    pool.tensor_tensor(n_mask[:], n_slope[:], mask[:, i, :], ALU.add).then_inc(nmask_ready, 1)

            run(pool, step)

        @block.scalar
        def _(act):
            act.dma_start(ident[:], identity).then_inc(small_loaded, 16)
            act.dma_start(a0_bc[:], a_self.partition_broadcast(P)).then_inc(small_loaded, 16)
            act.dma_start(a1_col[:], a_neigh).then_inc(small_loaded, 16)
            act.dma_start(wa_raw[:], w_att.rearrange("(k p) o -> p k o", p=P)).then_inc(small_loaded, 16)
            act.dma_start(degb[:, 0, :], bias.partition_broadcast(P)).then_inc(small_loaded, 16)
            act.wait_ge(weights_loaded, 16)
            act.copy(wl_hi[:], p_row[:, :, 0:2 * D]).then_inc(whi_ready, 1)
            act.wait_ge(small_loaded, 80)
            act.copy(wa_hi[:], wa_raw[:]).then_inc(whi_ready, 1)
            for t in range(T):
                act.wait_ge(adjt_loaded[t // 4], 16)
                act.copy(adjT[:, t, :], mask[:, t, :].bitcast(I32)).then_inc(adjt_ready, 1)

            def step(name, i, b, parity, half):
                if name in ("T1", "T2"):
                    for k in range(K):
                        g = A_GROUPS.index((name, i, k))
                        act.wait_ge(done[name], b * 4 + (2 * i + k + 1))
                        if name == "T1":
                            after(act, done["HH"], i + 1 - 2, 2, b)
                        else:
                            act.wait_ge(done["L0"], b * 8 + (4 * i + 4))
                        act.activation(hT_hi[:, k, 512 * i:512 * i + 512], ring[g % A_BANKS][:],
                                       ACT.Relu).then_inc(t_hi[name], 1)
                elif name == "L0":
                    g = A_GROUPS.index((name, i, 0))
                    act.wait_ge(done["L0"], b * 8 + (i + 1))
                    if i == 0:
                        after(act, done["AG"], 0, 4, b)
                    act.copy(mj_hi[:, i, :], ring[g % A_BANKS][:, D:2 * D]).then_inc(mjhi_ready, 1)
                elif name == "HH":
                    g = A_GROUPS.index((name, i, 0))
                    act.wait_ge(done["HH"], b * 2 + (i + 1))
                    after(act, done["TH"], i + 1 - 2, 2, b)
                    act.copy(hhT[:, i, :], ring[g % A_BANKS][:]).then_inc(hht_ready, 1)
                elif name == "NB":
                    g = A_GROUPS.index((name, i, 0))
                    act.wait_ge(done["NB"], b * 2 + (i + 1))
                    after(act, e_ready, 0, 8, b)
                    act.mul(n_slope[:, 512 * i:512 * i + 512], ring[g % A_BANKS][:], SLOPE)
                    act.copy(n_bc[:, 512 * i:512 * i + 512], ring[g % A_BANKS][:]).then_inc(nb_ready, 1)
                elif name == "HS":
                    g = A_GROUPS.index(("TH", i, 0))
                    act.wait_ge(xh_ready, b * 2 + (i + 1))
                    after(act, att_done, 0, 4, b)
                    act.copy(hh_hi[:, 4 * i:4 * i + 4, :],
                             ring[g % A_BANKS][:].rearrange("p (q h) -> p q h", q=4)).then_inc(hhhi_ready, 1)
                elif name == "SM":
                    if i in SHARED:
                        act.wait_ge(nb_ready, b * 2 + 2)
                        act.wait_ge(s_ready, b * 2 + 2)
                        after(act, tp_done, 2 * i - 2, 16, b)
                        act.activation(p_row[:, i % 2, :], n_bc[:], ACT.Relu, bias=s_rest[:, i:i + 1],
                                       scale=1.0 - SLOPE).then_inc(relu_ready, 1)
                    act.wait_ge(e_ready, b * 8 + (i + 1))
                    if i % 4 == 0:
                        after(act, out_ready, i // 4 + 1 - 2, 2, b)
                    act.activation(p_row[:, i % 2, :], p_row[:, i % 2, :], ACT.Exp, bias=neg_max[:, i:i + 1],
                                   scale=-1.0, accum_out=den[:, i:i + 1]).then_inc(p_ready, 1)
                elif name == "TP":
                    for h in range(2):
                        act.wait_ge(tp_done, b * 16 + (2 * i + h + 1))
                        if i % 4 == 0:
                            after(act, att_done, 2 * (i // 4) - 2 + h + 1, 4, b)
                        act.copy(pT_hi[:, 4 * h:4 * h + 4, P * (i % 4):P * (i % 4) + P],
                                 p_bank[(2 * i + h) % 4][:].rearrange("p (j i) -> p j i", j=4)
                                 ).then_inc(phi_ready, 1)
                elif name == "AT":
                    act.wait_ge(att_done, b * 4 + (2 * i + 2))
                    after(act, ob_done, i, 2, b)
                    if not (isinstance(b, int) and b == B - 1 and i == 1):
                        act.wait_ge(s_ready, b * 2 + (2 * i + 2))
                    act.copy(oT[:], o_bank[:]).then_inc(oT_ready, 1)

            run(act, step)

        @block.vector
        def _(dve):
            dve.wait_ge(whi_ready, 1)
            dve.tensor_tensor(wl_lo[:], p_row[:, :, 0:2 * D], wl_hi[:].bitcast(F32), ALU.subtract)
            dve.wait_ge(whi_ready, 2)
            dve.tensor_tensor(wa_lo[:], wa_raw[:], wa_hi[:].bitcast(F32), ALU.subtract).then_inc(w_ready, 1)

            def masks(h):
                dve.wait_ge(adj_loaded[h], 16)
                dve.tensor_reduce(deg[:, 4 * h:4 * h + 4], mask[:, 4 * h:4 * h + 4, :].bitcast(I32),
                                  mybir.AxisListType.X, ALU.add).then_inc(deg_ready, 1)
                dve.wait_ge(deg_ready, h + 1)
                dve.tensor_scalar(mask[:, 4 * h:4 * h + 4, :], mask[:, 4 * h:4 * h + 4, :].bitcast(I32),
                                  -NEG, NEG, ALU.mult, ALU.add).then_inc(mask_ready, 1)

            def step(name, i, b, parity, half):
                xt = xs[parity]
                first = isinstance(b, int) and b == 0
                if name in ("S1", "S2"):
                    if name == "S1":
                        dve.wait_ge(x_loaded[parity][i], half * 16 + 16)
                    else:
                        dve.wait_ge(x1_ready, b * 4 + (2 * i + 2))
                    which = int(name == "S2")
                    after(dve, moments_ready[name], i + 1 - 2, 2, b)
                    for q in range(4):
                        ins = dve.bn_stats(stats[:, which, i, q, :], xt[:, 4 * i + q, :])
                    ins.then_inc(bn_done[name], 1)
                    dve.wait_ge(bn_done[name], b * 2 + (i + 1))
                    if name == "S2":
                        dve.wait_ge(xn_ready["S1"], b * 2 + (i + 1))
                    else:
                        after(dve, xn_ready["S2"], i + 1 - 2, 2, b)
                    dve.sem_inc(dve_passed)
                    for q in range(4):
                        ins = dve.bn_aggr(moments[:, i, q, :], stats[:, which, i, q, :])
                    ins.then_inc(moments_ready[name], 1)
                    if first and name == "S1" and i == 1:
                        masks(0)
                        masks(1)
                        for t in range(T - 1, 0, -1):
                            ins = dve.tensor_scalar(degb[:, t, :], degb[:, 0, :], deg[:, t:t + 1], None, ALU.mult)
                        ins.then_inc(deg_ready, 1)
                        dve.wait_ge(deg_ready, 3)
                        dve.tensor_scalar(degb[:, 0, :], degb[:, 0, :], deg[:, 0:1], None,
                                          ALU.mult).then_inc(degb_ready, 1)
                elif name in ("T1", "T2"):
                    for k in range(K):
                        g = A_GROUPS.index((name, i, k))
                        dve.wait_ge(t_hi[name], b * 4 + (2 * i + k + 1))
                        dve.scalar_tensor_tensor(hT_lo[:, k, 512 * i:512 * i + 512], ring[g % A_BANKS][:], 0.0,
                                                 hT_hi[:, k, 512 * i:512 * i + 512].bitcast(F32), ALU.max,
                                                 ALU.subtract).then_inc(t_lo[name], 1)
                elif name == "L0":
                    bank = ring[A_GROUPS.index((name, i, 0)) % A_BANKS]
                    dve.wait_ge(mjhi_ready, b * 8 + (i + 1))
                    dve.tensor_tensor(mj_lo[:, i, :], bank[:, D:2 * D], mj_hi[:, i, :].bitcast(F32), ALU.subtract)
                    if i % 4 == 0:
                        dve.wait_ge(xb_ready, b * 2 + (i // 4 + 1))
                    dve.scalar_tensor_tensor(xt[:, i, :], bank[:, 0:D], deg[:, i:i + 1], xt[:, i, :], ALU.mult,
                                             ALU.add).then_inc(l0_read, 1)
                elif name == "AG":
                    bank = ring[A_GROUPS.index((name, i, 0)) % A_BANKS]
                    dve.wait_ge(done["AG"], b * 4 + (i + 1))
                    dve.tensor_tensor(xt[:, 2 * i:2 * i + 2, :], bank[:].rearrange("p (t d) -> p t d", t=2),
                                      xt[:, 2 * i:2 * i + 2, :], ALU.add).then_inc(x1_ready, 1)
                elif name == "TH":
                    bank = ring[A_GROUPS.index((name, i, 0)) % A_BANKS]
                    dve.wait_ge(done["TH"], b * 2 + (i + 1))
                    after(dve, p_ready, 0, 8, b)
                    after(dve, ob_done, -1, 2, b)
                    after(dve, s_ready, i, 2, b)
                    for q in range(4):
                        ins = dve.tensor_tensor_reduce(oT[:, H * q:H * q + H], bank[:, H * q:H * q + H], a0_bc[:], 1.0 - SLOPE, 0.0,
                                                       ALU.mult, ALU.add, s_rest[:, 4 * i + q:4 * i + q + 1])
                    ins.then_inc(s_ready, 1)
                    dve.wait_ge(xn_ready["S2"], b * 2 + (i + 1))
                    dve.tensor_tensor(xt[:, 4 * i:4 * i + 4, H:D], bank[:].rearrange("p (q h) -> p q h", q=4),
                                      xt[:, 4 * i:4 * i + 4, H:D], ALU.add).then_inc(xh_ready, 1)
                elif name == "HS":
                    bank = ring[A_GROUPS.index(("TH", i, 0)) % A_BANKS]
                    dve.wait_ge(hhhi_ready, b * 2 + (i + 1))
                    dve.tensor_tensor(hh_lo[:, 4 * i:4 * i + 4, :], bank[:].rearrange("p (q h) -> p q h", q=4),
                                      hh_hi[:, 4 * i:4 * i + 4, :].bitcast(F32), ALU.subtract).then_inc(hh_ready, 1)
                elif name == "SM":
                    row = p_row[:, i % 2, :]
                    if i in SHARED:
                        at = SHARED.index(i) + 1
                        dve.wait_ge(relu_ready, b * len(SHARED) + at)
                        dve.wait_ge(nmask_ready, b * len(SHARED) + at)
                        added = n_mask[:]
                    else:
                        dve.wait_ge(nb_ready, b * 2 + 2)
                        dve.wait_ge(s_ready, b * 2 + 2)
                        after(dve, tp_done, 2 * i - 2, 16, b)
                        dve.scalar_tensor_tensor(row, n_bc[:], s_rest[:, i:i + 1], n_slope[:], ALU.add,
                                                 ALU.max).then_inc(leaky_ready, 1)
                        dve.wait_ge(leaky_ready, b * (T - len(SHARED)) + (i + 1 - sum(j < i for j in SHARED)))
                        added = mask[:, i, :]
                    if first:
                        dve.wait_ge(mask_ready, 2)
                    dve.sem_inc(dve_passed)
                    dve.tensor_tensor_reduce(row, row, added, -1.0, FAR, ALU.add, ALU.min,
                                             neg_max[:, i:i + 1]).then_inc(e_ready, 1)
                elif name == "TP":
                    for h in range(2):
                        dve.wait_ge(phi_ready, b * 16 + (2 * i + h + 1))
                        part = (slice(None), slice(4 * h, 4 * h + 4), slice(P * (i % 4), P * (i % 4) + P))
                        dve.tensor_tensor(pT_lo[part], p_bank[(2 * i + h) % 4][:].rearrange("p (j i) -> p j i", j=4),
                                          pT_hi[part].bitcast(F32), ALU.subtract).then_inc(plo_ready, 1)
                elif name == "OB":
                    dve.wait_ge(p_ready, b * 8 + (4 * i + 4))
                    dve.reciprocal(rden[:, 4 * i:4 * i + 4], den[:, 4 * i:4 * i + 4]).then_inc(rden_ready, 1)
                    dve.wait_ge(rden_ready, b * 2 + (i + 1))
                    dve.wait_ge(ob_done, b * 2 + (i + 1))
                    for q in range(4):
                        t = 4 * i + q
                        ins = dve.scalar_tensor_tensor(xt[:, t, 0:H], o_bank[:, H * q:H * q + H], rden[:, t:t + 1],
                                                       xt[:, t, 0:H], ALU.mult, ALU.add)
                    ins.then_inc(out_ready, 1)

            run(dve, step)

        @block.tensor
        def _(pe):
            def bank_for(name, i, k, b):
                (s, j, l), earlier = ring_before(name, i, k)
                per = PER_BATCH[s]
                after(pe, ring_read[s], ordinal(s, j, l) - (per if earlier else 0), per, b)
                return ring[A_GROUPS.index((name, i, k)) % A_BANKS]

            def products(bank, pairs):
                for n, (w, m) in enumerate(pairs):
                    ins = nc.tensor.matmul(bank, w, m, start=n == 0, stop=n == len(pairs) - 1)
                return ins

            def step(name, i, b, parity, half):
                first = isinstance(b, int) and b == 0
                if name in ("T1", "T2"):
                    pe.wait_ge(xn_ready["S" + name[1]], b * 2 + (i + 1))
                    if first and name == "T1" and i == 0:
                        pe.wait_ge(small_loaded, 80)
                    for k in range(K):
                        bank = bank_for(name, i, k, b)
                        for q in range(4):
                            ins = nc.tensor.transpose(bank[:, P * q:P * q + P], xn[:, i, q, P * k:P * k + P], ident[:])
                        ins.then_inc(done[name], 1)
                elif name == "L0":
                    if i % 4 == 0:
                        pe.wait_ge(t_lo["T1"], b * 4 + (2 * (i // 4) + 2))
                    if first and i == 0:
                        pe.wait_ge(w_ready, 1)
                    bank = bank_for(name, i, 0, b)
                    rows = slice(P * i, P * i + P)
                    products(bank[:], [pair for k in range(K) for pair in (
                        (hT_hi[:, k, rows], wl_hi[:, k, :]), (hT_hi[:, k, rows], wl_lo[:, k, :]),
                        (hT_lo[:, k, rows], wl_hi[:, k, :]))]).then_inc(done[name], 1)
                elif name == "AG":
                    if i == 0:
                        pe.wait_ge(l0_read, b * 8 + 8)
                    if first and i == 0:
                        pe.wait_ge(adjt_ready, 8)
                    bank = bank_for(name, i, 0, b)
                    for n in range(2):
                        rows = slice(P * (2 * i + n), P * (2 * i + n) + P)
                        ins = products(bank[:, D * n:D * n + D], [
                            (adjT[:, j, rows], part[:, j, :]) for j in range(T) for part in (mj_hi, mj_lo)])
                    ins.then_inc(done[name], 1)
                elif name == "HH":
                    pe.wait_ge(t_lo["T2"], b * 4 + (2 * i + 2))
                    bank = bank_for(name, i, 0, b)
                    cols = slice(512 * i, 512 * i + 512)
                    products(bank[:], [pair for k in range(K) for pair in (
                        (wa_hi[:, k, :], hT_hi[:, k, cols]), (wa_hi[:, k, :], hT_lo[:, k, cols]),
                        (wa_lo[:, k, :], hT_hi[:, k, cols]))]).then_inc(done[name], 1)
                elif name == "NB":
                    pe.wait_ge(hht_ready, b * 2 + (i + 1))
                    bank = bank_for(name, i, 0, b)
                    products(bank[:], [(a1_col[:].broadcast_to([P, P]), hhT[:, i, :])]).then_inc(done[name], 1)
                elif name == "TH":
                    bank = bank_for(name, i, 0, b)
                    for q in range(4):
                        ins = nc.tensor.transpose(bank[:, P * q:P * q + P], hhT[:, i, P * q:P * q + P], ident[:])
                    ins.then_inc(done[name], 1)
                elif name == "TP":
                    pe.wait_ge(p_ready, b * 8 + (i + 1))
                    for h in range(2):
                        after(pe, plo_ready, 2 * i + h - 3, 16, b)
                        for q in range(4):
                            j = 4 * h + q
                            ins = nc.tensor.transpose(p_bank[(2 * i + h) % 4][:, P * q:P * q + P],
                                                      p_row[:, i % 2, P * j:P * j + P], ident[:])
                        ins.then_inc(tp_done, 1)
                elif name == "AT":
                    if i == 0:
                        pe.wait_ge(hh_ready, b * 2 + 2)
                    pe.wait_ge(plo_ready, b * 16 + (8 * i + 8))
                    after(pe, out_ready, i, 2, b)
                    for j in range(T):
                        for n, (w, m) in enumerate(((hh_hi, pT_hi), (hh_hi, pT_lo), (hh_lo, pT_hi))):
                            ins = nc.tensor.matmul(o_bank[:], w[:, j, :], m[:, j, :], start=j + n == 0,
                                                   stop=j == T - 1 and n == 2)
                        if j % 4 == 3:
                            ins.then_inc(att_done, 1)
                elif name == "OB":
                    pe.wait_ge(oT_ready, b * 2 + (i + 1))
                    for q in range(4):
                        ins = nc.tensor.transpose(o_bank[:, P * q:P * q + P], oT[:, P * q:P * q + P], ident[:])
                    ins.then_inc(ob_done, 1)

            run(pe, step)


def kernel(x, adj, L0_gnn_W, L0_gnn_b, L1_gnn_W, L1_gnn_a):
    import numpy as np
    import concourse.bacc as bacc
    from concourse.bass_utils import run_bass_kernel_spmd

    t = adj.shape[0] // P
    tiled = np.asarray(adj).reshape(P, t, P, t)
    din = x.shape[-1]
    w = np.asarray(L0_gnn_W)
    arrays = {
        "x": np.asarray(x),
        "adj": tiled.transpose(0, 1, 3, 2).reshape(P, t, -1),
        "adj_t": tiled.transpose(2, 3, 1, 0).reshape(P, t, -1),
        "w_cat_t": np.concatenate([w[:, :din].T, w[:, din:].T], axis=1),
        "bias": np.asarray(L0_gnn_b),
        "w_att": np.asarray(L1_gnn_W),
        "a_self": np.asarray(L1_gnn_a)[0, :, 0],
        "a_neigh": np.asarray(L1_gnn_a)[1],
        "identity": np.eye(P, dtype=np.float32),
    }
    arrays = {f"in_{k}": np.ascontiguousarray(v) for k, v in arrays.items()}
    nc = bacc.Bacc("TRN2", target_bir_lowering=False, num_devices=1)
    args = [nc.dram_tensor(k, v.shape, mybir.dt.from_np(v.dtype), kind="ExternalInput").ap() for k, v in arrays.items()]
    out = nc.dram_tensor("out", x.shape, F32, kind="ExternalOutput").ap()
    build(nc, *args, out)
    result = run_bass_kernel_spmd(nc, [arrays], core_ids=[0])
    return result.results[0]["out"]
```

```python
from contextlib import ExitStack

import concourse.bass as bass
from concourse import mybir

F32 = mybir.dt.float32
F32R = mybir.dt.float32r
I32 = mybir.dt.int32
ALU = mybir.AluOpType
ACT = mybir.ActivationFunctionType

P = 128
NEG = -1.0e9
SLOPE = 0.2
EPS = 1e-5
FAR = 3.0e38

TENSOR_FIRST = """
    TRANSPOSE1.0.0 TRANSPOSE1.0.1 TRANSPOSE1.1.0 TRANSPOSE1.1.1 LINEAR.0 LINEAR.1 LINEAR.2 LINEAR.3 LINEAR.4
    LINEAR.5 LINEAR.6 LINEAR.7 AGGREGATE.0.0 AGGREGATE.0.1 AGGREGATE.1.0 AGGREGATE.1.1 AGGREGATE.2.0
    AGGREGATE.2.1 AGGREGATE.3.0 AGGREGATE.3.1 TRANSPOSE2.0.0 TRANSPOSE2.0.1 TRANSPOSE2.1.0 TRANSPOSE2.1.1 HH.0
    HH.1 N_ROW.0 HH_BACK.0 N_ROW.1 HH_BACK.1 TRANSPOSE1.0.0> P_BACK.0.0 P_BACK.0.1 TRANSPOSE1.0.1>
    TRANSPOSE1.1.0> TRANSPOSE1.1.1> P_BACK.1.0 P_BACK.1.1 LINEAR.0> LINEAR.1> LINEAR.2> LINEAR.3> LINEAR.4>
    LINEAR.5> LINEAR.6> LINEAR.7> P_BACK.2.0 P_BACK.2.1 P_BACK.3.0 P_BACK.3.1 AGGREGATE.0.0> AGGREGATE.0.1>
    AGGREGATE.1.0> AGGREGATE.1.1> P_BACK.4.0 P_BACK.4.1 AGGREGATE.2.0> AGGREGATE.2.1> AGGREGATE.3.0>
    AGGREGATE.3.1> P_BACK.5.0 TRANSPOSE2.0.0> TRANSPOSE2.0.1> P_BACK.5.1 ATTEND.0.0 ATTEND.0.1 P_BACK.6.0
    TRANSPOSE2.1.0> TRANSPOSE2.1.1> HH.0> P_BACK.6.1 O_BACK.0 HH.1> P_BACK.7.0 N_ROW.0> HH_BACK.0> N_ROW.1>
    HH_BACK.1> P_BACK.7.1 ATTEND.1.0 ATTEND.1.1
"""
TENSOR_ORDER = """
    TRANSPOSE1.0.0> P_BACK.0.0 P_BACK.0.1 O_BACK.1< TRANSPOSE1.0.1> TRANSPOSE1.1.0> TRANSPOSE1.1.1> P_BACK.1.0
    P_BACK.1.1 LINEAR.0> LINEAR.1> LINEAR.2> LINEAR.3> LINEAR.4> LINEAR.5> LINEAR.6> LINEAR.7> P_BACK.2.0
    P_BACK.2.1 P_BACK.3.0 P_BACK.3.1 AGGREGATE.0.0> AGGREGATE.0.1> AGGREGATE.1.0> AGGREGATE.1.1> P_BACK.4.0
    P_BACK.4.1 AGGREGATE.2.0> AGGREGATE.2.1> AGGREGATE.3.0> AGGREGATE.3.1> P_BACK.5.0 TRANSPOSE2.0.0>
    TRANSPOSE2.0.1> P_BACK.5.1 ATTEND.0.0 ATTEND.0.1 P_BACK.6.0 TRANSPOSE2.1.0> TRANSPOSE2.1.1> HH.0> P_BACK.6.1
    O_BACK.0 HH.1> P_BACK.7.0 N_ROW.0> HH_BACK.0> N_ROW.1> HH_BACK.1> P_BACK.7.1 ATTEND.1.0 ATTEND.1.1
"""
TENSOR_LAST = """
    P_BACK.0.0 P_BACK.0.1 P_BACK.1.0 P_BACK.1.1 WARM O_BACK.1< P_BACK.2.0 P_BACK.2.1 WARM P_BACK.3.0 P_BACK.3.1
    P_BACK.4.0 P_BACK.4.1 ATTEND.0.0 P_BACK.5.0 P_BACK.5.1 ATTEND.0.1 WARM P_BACK.6.0 P_BACK.6.1 O_BACK.0 WARM
    P_BACK.7.0 P_BACK.7.1 ATTEND.1.0 ATTEND.1.1 O_BACK.1
"""
VECTOR_FIRST = """
    STATS1.0 STATS1.1 LO1.0.0 LO1.0.1 W_LO LO1.1.0 LO1.1.1 MJ_LO_MI.0 MJ_LO_MI.1 MJ_LO_MI.2 MJ_LO_MI.3 DEG.0
    MJ_LO_MI.4 DEG.1 MJ_LO_MI.5 MJ_LO_MI.6 MJ_LO_MI.7 DEG.2 MASK.0 DEG_MI.0 DEG.3 DEG_MI.1 DEG.4 X1.0 DEG.5 X1.1
    DEG_MI.2 DEG.6 STATS2.0 DEG.7 X1.2 DEG_MI.3 X1.3 STATS2.1 MASK.2 WA_LO LO2.0.0 STATS1.0> LO2.0.1 STATS1.1>
    MASK.4 LO2.1.0 LO2.1.1 MASK.6 S_ADD.0 S_ADD.1 SCORES.0 SCORES.1 HH_LO.0 HH_LO.1 LO1.0.0> LO1.0.1> P_LO.0.0
    LO1.1.0> LO1.1.1> P_LO.0.1 MJ_LO_MI.0> SCORES.2 MJ_LO_MI.1> P_LO.1.0 MJ_LO_MI.2> MJ_LO_MI.3> MJ_LO_MI.4>
    SCORES.3 MJ_LO_MI.5> P_LO.1.1 MJ_LO_MI.6> MJ_LO_MI.7> P_LO.2.0
"""
VECTOR_ORDER = """
    STATS1.0> P_LO.2.1< SCORES.4< P_LO.3.0< X1.0 SCORES.5< X1.1 STATS2.0 STATS1.1> SCORES.6< P_LO.3.1< X1.2 X1.3
    STATS2.1 SCORES.7< P_LO.4.0< LO2.0.0 LO2.0.1 P_LO.4.1< P_LO.5.0< LO2.1.0 LO2.1.1 P_LO.5.1< OUT.0< P_LO.6.0<
    P_LO.6.1< P_LO.7.0< S_ADD.0 S_ADD.1 P_LO.7.1< SCORES.0 SCORES.1 HH_LO.0 HH_LO.1 LO1.0.0> LO1.0.1> P_LO.0.0
    LO1.1.0> LO1.1.1> P_LO.0.1 MJ_LO_MI.0> SCORES.2 MJ_LO_MI.1> P_LO.1.0 MJ_LO_MI.2> MJ_LO_MI.3> MJ_LO_MI.4>
    SCORES.3 MJ_LO_MI.5> P_LO.1.1 MJ_LO_MI.6> MJ_LO_MI.7> OUT.1< P_LO.2.0
"""
VECTOR_LAST = """
    P_LO.2.1< SCORES.4< P_LO.3.0< X1.0 SCORES.5< X1.1 STATS2.0 SCORES.6< P_LO.3.1< X1.2 X1.3 STATS2.1 SCORES.7<
    P_LO.4.0< LO2.0.0 LO2.0.1 P_LO.4.1< P_LO.5.0< LO2.1.0 LO2.1.1 P_LO.5.1< OUT.0< P_LO.6.0< P_LO.6.1< P_LO.7.0<
    S_ADD.0 S_ADD.1 P_LO.7.1< SCORES.0 SCORES.1 P_LO.0.0 P_LO.0.1 SCORES.2 SCORES.3 OUT.1< HH_LO.0 P_LO.1.0
    SCORES.4 P_LO.1.1 P_LO.2.0 P_LO.2.1 HH_LO.1 P_LO.3.0 SCORES.5 P_LO.3.1 SCORES.6 P_LO.4.0 SCORES.7 P_LO.4.1
    P_LO.5.0 P_LO.5.1 OUT.0 P_LO.6.0 P_LO.6.1 P_LO.7.0 P_LO.7.1 OUT.1
"""
SCALAR_FIRST = """
    W_HI ADJ_T.0 HI1.0.0 WA_HI ADJ_T.1 HI1.0.1 ADJ_T.2 HI1.1.0 ADJ_T.3 ADJ_T.4 HI1.1.1 MJ_HI.0 MJ_HI.1 ADJ_T.5
    MJ_HI.2 MJ_HI.3 MJ_HI.4 ADJ_T.6 MJ_HI.5 MJ_HI.6 ADJ_T.7 MJ_HI.7 DEG_BIAS HI2.0.0 HI2.0.1 HI2.1.0 HI2.1.1
    HHT.0 HHT.1 EXPAND.1 N.0 N.1 RELU.0 RELU.1 EXP.0 HH_HI.0 HH_HI.1 HI1.0.0> EXP.1 HI1.0.1> P_HI.0.0 HI1.1.0>
    HI1.1.1> P_HI.0.1 MJ_HI.0> RELU.2 EXPAND.3 MJ_HI.1> P_HI.1.0 MJ_HI.2> MJ_HI.3> RELU.3 MJ_HI.4> EXP.2
    MJ_HI.5> P_HI.1.1 MJ_HI.6> EXP.3 MJ_HI.7> P_HI.2.0 RELU.4 RELU.5 EXPAND.5 P_HI.2.1 P_HI.3.0 P_HI.3.1 EXP.4
    EXP.5 EXPAND.7 RELU.6 HI2.0.0> EXP.6 RELU.7 P_HI.4.0 HI2.0.1> EXP.7 P_HI.4.1 P_HI.5.0 HI2.1.0> HI2.1.1> OT.0
    P_HI.5.1 HHT.0> P_HI.6.0 P_HI.6.1 P_HI.7.0 HHT.1> N.0> EXPAND.1> N.1> P_HI.7.1
"""
SCALAR_ORDER = """
    RELU.0 RELU.1 EXP.0 HH_HI.0 HH_HI.1 OT.1< HI1.0.0> EXP.1 HI1.0.1> P_HI.0.0 HI1.1.0> HI1.1.1> P_HI.0.1
    MJ_HI.0> RELU.2 EXPAND.3 MJ_HI.1> P_HI.1.0 MJ_HI.2> MJ_HI.3> RELU.3 MJ_HI.4> EXP.2 MJ_HI.5> P_HI.1.1
    MJ_HI.6> EXP.3 MJ_HI.7> P_HI.2.0 RELU.4 RELU.5 EXPAND.5 P_HI.2.1 P_HI.3.0 P_HI.3.1 EXP.4 EXP.5 EXPAND.7
    RELU.6 HI2.0.0> EXP.6 RELU.7 P_HI.4.0 HI2.0.1> EXP.7 P_HI.4.1 P_HI.5.0 HI2.1.0> HI2.1.1> OT.0 P_HI.5.1
    HHT.0> P_HI.6.0 P_HI.6.1 P_HI.7.0 HHT.1> N.0> EXPAND.1> N.1> P_HI.7.1
"""
SCALAR_LAST = """
    RELU.0 RELU.1 EXP.0 OT.1< EXPAND.3 HH_HI.0 P_HI.0.0 P_HI.0.1 EXP.1 RELU.2 HH_HI.1 P_HI.1.0 RELU.3 EXP.2
    P_HI.1.1 EXPAND.5 RELU.4 EXP.3 P_HI.2.0 P_HI.2.1 EXP.4 P_HI.3.0 RELU.5 RELU.6 P_HI.3.1 EXP.5 EXPAND.7
    P_HI.4.0 RELU.7 EXP.6 OT.0 P_HI.4.1 P_HI.5.0 P_HI.5.1 P_HI.6.0 EXP.7 P_HI.6.1 P_HI.7.0 P_HI.7.1 OT.1
"""
GPSIMD_FIRST = """
    NORM1.0 NORM1.1 KEEP.1 KEEP.3 KEEP.5 KEEP.7 NORM2.0 NORM2.1 NORM1.0> NORM1.1> N_MASK.0 N_MASK.1 ADD_BIAS.0>
    N_MASK.2 ADD_BIAS.1> N_MASK.3 N_MASK.4 N_MASK.5 N_MASK.6 NORM2.0> N_MASK.7 NORM2.1>
"""
GPSIMD_ORDER = """
    NORM1.0> NORM1.1> N_MASK.0 N_MASK.1 ADD_BIAS.0> N_MASK.2 ADD_BIAS.1> N_MASK.3 N_MASK.4 N_MASK.5 N_MASK.6
    NORM2.0> N_MASK.7 NORM2.1>
"""
GPSIMD_LAST = """
    N_MASK.0 N_MASK.1 N_MASK.2 N_MASK.3 N_MASK.4 N_MASK.5 N_MASK.6 N_MASK.7
"""

def steps(order):
    for word in order.split():
        ahead = word.count(">") - word.count("<")
        name, *numbers = word.rstrip("<>").split(".")
        i, k = [int(n) for n in numbers + ["0", "0"]][:2]
        yield name, i, k, ahead


PER_BATCH = {"TRANSPOSE1": 4, "LINEAR": 8, "AGGREGATE": 4, "TRANSPOSE2": 4, "HH": 2, "N_ROW": 2, "HH_BACK": 2}
A_GROUPS = [(name, i, k) for name, i, k, _ in steps(TENSOR_ORDER)
            if name in PER_BATCH and (k == 0 or name != "AGGREGATE")]
A_BANKS = 3
X_BUFFERS = 3
A_SLOTS = -(-len(A_GROUPS) // A_BANKS) * A_BANKS


def ring_before(group):
    at = A_GROUPS.index(group) - A_BANKS
    earlier = at < 0
    at %= A_SLOTS
    while at >= len(A_GROUPS):
        at -= A_BANKS
    return A_GROUPS[at], earlier


def ordinal(name, i, k):
    return 1 + (2 * i + k if name.startswith("TRANSPOSE") else i)


def build(nc, x, adj, adj_t, w_cat_t, bias, w_att, a_self, a_neigh, identity, out):
    B, _, D = x.shape
    T = 8
    N = P * T
    H = D // 2
    K = D // P
    assert D == 2 * P and w_cat_t.shape == (D, 2 * D) and w_att.shape == (D, H)

    x_rows = x.rearrange("b (p t) d -> b p t d", p=P)
    out_rows = out.rearrange("b (p t) d -> b p t d", p=P)

    ctx = ExitStack()
    with ctx:
        def sb(name, shape, dt=F32):
            return ctx.enter_context(nc.sbuf_tensor(name, shape, dt))

        def sem(name):
            return ctx.enter_context(nc.semaphore(name))

        adjT = sb("adjT", [P, T, N], F32R)
        mask = sb("mask", [P, T // 2, N])
        adj_kept = sb("adj_kept", [P, T // 2, N], mybir.dt.bfloat16)
        wl_hi = sb("wl_hi", [P, K, 2 * D], F32R)
        wl_lo = sb("wl_lo", [P, K, 2 * D], F32R)
        wa_hi = sb("wa_hi", [P, K, H], F32R)
        wa_lo = sb("wa_lo", [P, K, H], F32R)
        a0_bc = sb("a0_bc", [P, H])
        a1_col = sb("a1_col", [P, 1])
        ident = sb("ident", [P, P])
        degb = sb("degb", [P, T, D])
        deg = sb("deg", [P, T])
        xs = [sb(f"x{i}", [P, T, D]) for i in range(X_BUFFERS)]
        xn = sb("xn", [P, 2, 4, D])
        stats = sb("stats", [P, 2, 2, 4, 6])
        moments = sb("moments", [P, 2, 2, 4, 2])
        neg_mean = sb("neg_mean", [P, 2, 2, 4])
        rstd = sb("rstd", [P, 2, 2, 4])
        minus_half = sb("minus_half", [P, 4])
        hT_hi = sb("hT_hi", [P, K, N], F32R)
        hT_lo = sb("hT_lo", [P, K, N], F32R)
        mj_hi = sb("mj_hi", [P, T, D], F32R)
        mj_lo = sb("mj_lo", [P, T, D], F32R)
        hhT = sb("hhT", [P, 2, N // 2])
        hh_hi = sb("hh_hi", [P, T, H], F32R)
        hh_lo = sb("hh_lo", [P, T, H], F32R)
        n_slope = sb("n_slope", [P, N])
        s_rest = sb("s_rest", [P, T])
        s_products = sb("s_products", [P, 4, H])
        neg_max = sb("neg_max", [P, T])
        den = sb("den", [P, T])
        rden = sb("rden", [P, T])
        p_row = sb("p_row", [P, 2, N])
        n_mask = sb("n_mask", [P, 2, N])
        pT_hi = sb("pT_hi", [P, T, N // 2], F32R)
        pT_lo = sb("pT_lo", [P, T, N // 2], F32R)
        in_x = [xs[b][:].rearrange("p (a t) d -> p a (t d)", a=2)[:, a, :].bitcast(I32)
                for b in (1, 2) for a in range(2)]
        in_mask = [mask[:, t, :].bitcast(I32) for t in range(T // 2)]
        adj_t_raw = in_mask[2:] + in_x + [n_slope[:].bitcast(I32), n_mask[:, 1, :].bitcast(I32)]
        adj_raw = [(in_x if t % 2 else in_mask)[t // 2] for t in range(T)]
        place_read = [0, 3, 3, 4, 4, 5, 5, 6]
        wa_raw = n_mask[:, 0, 0:K * H].rearrange("p (k h) -> p k h", k=K)
        wl_raw = p_row[:, :, 0:2 * D]
        mi_bias = p_row[:].rearrange("p r (t d) -> p (r t) d", d=D)
        oT = sb("oT", [P, N // 2])

        ring = [ctx.enter_context(nc.psum_tensor(f"ring{i}", [P, 512], F32)) for i in range(A_BANKS)]
        p_bank = [ctx.enter_context(nc.psum_tensor(f"p_bank{i}", [P, 512], F32)) for i in range(4)]
        o_bank = ctx.enter_context(nc.psum_tensor("o_bank", [P, 512], F32))

        x_loaded = [[sem(f"x_loaded{i}{c}") for c in range(2)] for i in range(X_BUFFERS)]
        adjt_loaded = [sem(f"adjt_loaded{t}") for t in range(T)]
        adj_loaded = [sem(f"adj_loaded{t}") for t in range(T)]
        weights_loaded = sem("weights_loaded")
        ident_loaded = sem("ident_loaded")
        small_loaded = sem("small_loaded")
        att_loaded = sem("att_loaded")
        stored = sem("stored")
        adjt_ready = sem("adjt_ready")
        mask_ready = sem("mask_ready")
        kept_ready = sem("kept_ready")
        deg_ready = sem("deg_ready")
        degb_ready = sem("degb_ready")
        wl_hi_ready = sem("wl_hi_ready")
        wa_hi_ready = sem("wa_hi_ready")
        wl_ready = sem("wl_ready")
        wa_ready = sem("wa_ready")
        half_ready = sem("half_ready")
        done = {s: sem(f"{s}_done") for s in PER_BATCH}
        tp_done = sem("tp_done")
        att_done = sem("att_done")
        ob_done = sem("ob_done")
        t_lo = {n: sem(f"t{n}_lo") for n in "12"}
        l0_read = sem("l0_read")
        x1_ready = sem("x1_ready")
        hht_ready = sem("hht_ready")
        nb_ready = sem("nb_ready")
        hh_ready = sem("hh_ready")
        ring_read = {"TRANSPOSE1": t_lo["1"], "TRANSPOSE2": t_lo["2"], "LINEAR": l0_read, "AGGREGATE": x1_ready,
                     "HH": hht_ready, "N_ROW": nb_ready, "HH_BACK": hh_ready}
        bn_done = {n: sem(f"bn{n}_done") for n in "12"}
        moments_ready = {n: sem(f"moments{n}_ready") for n in "12"}
        negated = {n: sem(f"negated{n}") for n in "12"}
        rstd_ready = {n: sem(f"rstd{n}_ready") for n in "12"}
        xn_ready = {n: sem(f"xn{n}_ready") for n in "12"}
        t_hi = {n: sem(f"t{n}_hi") for n in "12"}
        xb_ready = sem("xb_ready")
        deg_mi_ready = sem("deg_mi_ready")
        mjhi_ready = sem("mjhi_ready")
        s_ready = sem("s_ready")
        xh_ready = sem("xh_ready")
        hhhi_ready = sem("hhhi_ready")
        relu_ready = sem("relu_ready")
        expanded = sem("expanded")
        nmask_ready = sem("nmask_ready")
        e_ready = sem("e_ready")
        p_ready = sem("p_ready")
        phi_ready = sem("phi_ready")
        plo_ready = sem("plo_ready")
        oT_ready = sem("oT_ready")
        rden_ready = sem("rden_ready")
        out_ready = sem("out_ready")
        dve_passed = sem("dve_passed")
        pool_passed = sem("pool_passed")

        block = ctx.enter_context(nc.Block())

        def after(eng, s, n, per, b):
            if isinstance(b, int) and b * per + n <= 0:
                return
            eng.wait_ge(s, b * per + n)

        def bank_of(name, i, k=0):
            return ring[A_GROUPS.index((name, i, k)) % A_BANKS]

        def run(eng, first, order, last, step):
            order = list(steps(order))

            def alone(it, order):
                for name, i, k, ahead in order:
                    step(name, i, k, it + ahead, (it + ahead) % 3, (it + ahead) // 3)

            alone(0, steps(first))
            with eng.Fori(0, (B - 2) // 3) as t:
                for it in (1, 2, 3):
                    for name, i, k, ahead in order:
                        n = it + ahead
                        step(name, i, k, t * 3 + n if n else t * 3, n % 3, t + n // 3 if n // 3 else t)
            alone(B - 1, steps(last))

        @block.sync
        def _(sp):
            def load_x(b, slot, c):
                sp.dma_start(xs[slot][:, 4 * c:4 * c + 4, :],
                             x_rows[b, :, 4 * c:4 * c + 4, :]).then_inc(x_loaded[slot][c], 16)

            def store_out(b, slot, c):
                sp.wait_ge(out_ready, b * 2 + (c + 1))
                sp.dma_start(out_rows[b, :, 4 * c:4 * c + 4, :],
                             xs[slot][:, 4 * c:4 * c + 4, :]).then_inc(stored, 16)
                sp.wait_ge(stored, b * 32 + (16 * c + 16))

            load_x(0, 0, 0)
            sp.dma_start(wl_raw, w_cat_t.rearrange("(k p) o -> p k o", p=P)).then_inc(weights_loaded, 16)
            load_x(0, 0, 1)
            for t in range(T):
                sp.dma_start(adj_t_raw[t], adj_t[:, t, :]).then_inc(adjt_loaded[t], 16)
            for t in range(T):
                if place_read[t]:
                    sp.wait_ge(adjt_ready, place_read[t])
                sp.dma_start(adj_raw[t], adj[:, t, :]).then_inc(adj_loaded[t], 16)
            for b in (1, 2):
                sp.wait_ge(deg_ready, 4 * b)
                sp.wait_ge(kept_ready, 2 * b)
                for c in range(2):
                    load_x(b, b, c)
            for b in (0, 1):
                for c in range(2):
                    store_out(b, b, c)
                    load_x(b + 3, b, c)
            with sp.Fori(0, (B - 5) // 3) as t:
                for n in (2, 3, 4):
                    for c in range(2):
                        store_out(t * 3 + n, n % 3, c)
                        load_x(t * 3 + (n + 3), n % 3, c)
            for b in range(B - 3, B):
                for c in range(2):
                    store_out(b, b % 3, c)

        @block.gpsimd
        def _(pool):
            pool.memset(minus_half[:], -0.5).then_inc(half_ready, 1)
            pool.wait_ge(half_ready, 1)

            def step(name, i, k, b, slot, turn):
                if name in ("NORM1", "NORM2"):
                    n = name[-1]
                    which = int(n) - 1
                    pool.wait_ge(moments_ready[n], b * 2 + (i + 1))
                    after(pool, xn_ready[n], i + 1 - 2, 2, b)
                    pool.sem_inc(pool_passed)
                    pool.tensor_scalar(rstd[:, which, i, :], moments[:, which, i, :, 1], EPS, 1.0, ALU.add,
                                       ALU.mult).then_inc(negated[n], 1)
                    pool.tensor_scalar(neg_mean[:, which, i, :], moments[:, which, i, :, 0], -1.0, 0.0, ALU.mult,
                                       ALU.add).then_inc(negated[n], 1)
                    pool.wait_ge(negated[n], b * 4 + (2 * i + 2))
                    pool.tensor_tensor(rstd[:, which, i, :], rstd[:, which, i, :], minus_half[:],
                                       ALU.pow).then_inc(rstd_ready[n], 1)
                    pool.wait_ge(rstd_ready[n], b * 2 + (i + 1))
                    if which:
                        pool.wait_ge(done["TRANSPOSE1"], b * 4 + (2 * i + 2))
                    else:
                        after(pool, done["TRANSPOSE2"], 2 * i + 2 - 4, 4, b)
                    pool.sem_inc(pool_passed)
                    for q in range(4):
                        ins = pool.tensor_scalar(xn[:, i, q, :], xs[slot][:, 4 * i + q, :],
                                                 neg_mean[:, which, i, q:q + 1], rstd[:, which, i, q:q + 1],
                                                 ALU.add, ALU.mult)
                    ins.then_inc(xn_ready[n], 1)
                elif name == "KEEP":
                    pool.wait_ge(adj_loaded[i], 16)
                    pool.tensor_scalar(adj_kept[:, i // 2, :], adj_raw[i], 1.0, 0.0, ALU.mult,
                                       ALU.add).then_inc(kept_ready, 1)
                elif name == "ADD_BIAS":
                    rows = xs[slot][:, 4 * i:4 * i + 4, :]
                    pool.wait_ge(xn_ready["1"], b * 2 + (i + 1))
                    if isinstance(b, int) and b == 1 and i == 0:
                        pool.wait_ge(degb_ready, 1)
                    pool.tensor_tensor(rows, rows, degb[:, 4 * i:4 * i + 4, :], ALU.add).then_inc(xb_ready, 1)
                else:
                    row = n_mask[:, i % 2, :]
                    pool.wait_ge(nb_ready, b * 2 + 2)
                    if i % 2:
                        pool.wait_ge(expanded, b * 4 + (i // 2 + 1))
                        pool.sem_inc(pool_passed)
                        pool.tensor_tensor(row, row, n_slope[:], ALU.add).then_inc(nmask_ready, 1)
                    else:
                        after(pool, e_ready, i - 1, 8, b)
                        if isinstance(b, int) and b == 0 and i == 0:
                            pool.wait_ge(mask_ready, 4)
                        pool.tensor_tensor(row, n_slope[:], mask[:, i // 2, :], ALU.add).then_inc(nmask_ready, 1)

            run(pool, GPSIMD_FIRST, GPSIMD_ORDER, GPSIMD_LAST, step)

        @block.scalar
        def _(act):
            act.dma_start(ident[:], identity).then_inc(ident_loaded, 16)
            act.dma_start(wa_raw, w_att.rearrange("(k p) o -> p k o", p=P)).then_inc(small_loaded, 16)
            act.dma_start(degb[:, 0, :], bias.partition_broadcast(P)).then_inc(small_loaded, 16)
            act.dma_start(a0_bc[:], a_self.partition_broadcast(P)).then_inc(att_loaded, 16)
            act.dma_start(a1_col[:], a_neigh).then_inc(att_loaded, 16)

            def step(name, i, k, b, slot, turn):
                first = isinstance(b, int) and b == 0
                if name == "W_HI":
                    act.wait_ge(weights_loaded, 16)
                    act.copy(wl_hi[:], wl_raw).then_inc(wl_hi_ready, 1)
                elif name == "WA_HI":
                    act.wait_ge(small_loaded, 32)
                    act.copy(wa_hi[:], wa_raw).then_inc(wa_hi_ready, 1)
                elif name == "ADJ_T":
                    act.wait_ge(adjt_loaded[i], 16)
                    act.copy(adjT[:, i, :], adj_t_raw[i]).then_inc(adjt_ready, 1)
                elif name == "DEG_BIAS":
                    act.wait_ge(deg_ready, 8)
                    act.wait_ge(l0_read, 8)
                    for t in range(T - 1, -1, -1):
                        ins = act.mul(degb[:, t, :], degb[:, 0, :], deg[:, t:t + 1])
                    ins.then_inc(degb_ready, 1)
                elif name in ("HI1", "HI2"):
                    n = name[-1]
                    act.wait_ge(done["TRANSPOSE" + n], b * 4 + (2 * i + k + 1))
                    if n == "1":
                        after(act, done["HH"], i + 1 - 2, 2, b)
                    else:
                        act.wait_ge(done["LINEAR"], b * 8 + (4 * i + 4))
                    act.activation(hT_hi[:, k, 512 * i:512 * i + 512], bank_of("TRANSPOSE" + n, i, k)[:],
                                   ACT.Relu).then_inc(t_hi[n], 1)
                elif name == "MJ_HI":
                    act.wait_ge(done["LINEAR"], b * 8 + (i + 1))
                    if i == 0:
                        after(act, done["AGGREGATE"], 0, 4, b)
                    act.copy(mj_hi[:, i, :], bank_of("LINEAR", i)[:, D:2 * D]).then_inc(mjhi_ready, 1)
                elif name == "HHT":
                    act.wait_ge(done["HH"], b * 2 + (i + 1))
                    after(act, done["HH_BACK"], i + 1 - 2, 2, b)
                    act.copy(hhT[:, i, :], bank_of("HH", i)[:]).then_inc(hht_ready, 1)
                elif name == "N":
                    cols = slice(512 * i, 512 * i + 512)
                    act.wait_ge(done["N_ROW"], b * 2 + (i + 1))
                    if i == 0:
                        after(act, relu_ready, 0, 8, b)
                        after(act, nmask_ready, 0, 8, b)
                    act.mul(n_slope[:, cols], bank_of("N_ROW", i)[:], SLOPE).then_inc(nb_ready, 1)
                elif name == "HH_HI":
                    act.wait_ge(xh_ready, b * 2 + (i + 1))
                    if i == 0:
                        after(act, att_done, 0, 4, b)
                    act.copy(hh_hi[:, 4 * i:4 * i + 4, :],
                             bank_of("HH_BACK", i)[:].rearrange("p (q h) -> p q h", q=4)).then_inc(hhhi_ready, 1)
                elif name == "RELU":
                    act.wait_ge(nb_ready, b * 2 + 2)
                    act.wait_ge(s_ready, b * 2 + 2)
                    after(act, tp_done, 2 * (i + 1 - 2), 16, b)
                    act.activation(p_row[:, i % 2, :], n_slope[:], ACT.Relu, bias=s_rest[:, i:i + 1],
                                   scale=(1.0 - SLOPE) / SLOPE).then_inc(relu_ready, 1)
                elif name == "EXPAND":
                    if first and i == 1:
                        act.wait_ge(kept_ready, 4)
                    after(act, e_ready, i - 1, 8, b)
                    act.activation(n_mask[:, 1, :], adj_kept[:, i // 2, :], ACT.Copy, bias=NEG,
                                   scale=-NEG).then_inc(expanded, 1)
                elif name == "EXP":
                    act.wait_ge(e_ready, b * 8 + (i + 1))
                    if i % 4 == 0:
                        after(act, out_ready, i // 4 + 1 - 2, 2, b)
                    row = p_row[:, i % 2, :]
                    act.activation(row, row, ACT.Exp, bias=neg_max[:, i:i + 1], scale=-1.0,
                                   accum_out=den[:, i:i + 1]).then_inc(p_ready, 1)
                elif name == "P_HI":
                    act.wait_ge(tp_done, b * 16 + (2 * i + k + 1))
                    if i % 4 == 0:
                        after(act, att_done, 2 * (i // 4) - 2 + k + 1, 4, b)
                    act.copy(pT_hi[:, 4 * k:4 * k + 4, P * (i % 4):P * (i % 4) + P],
                             p_bank[(2 * i + k) % 4][:].rearrange("p (j i) -> p j i", j=4)).then_inc(phi_ready, 1)
                else:
                    act.wait_ge(att_done, b * 4 + (2 * i + 2))
                    after(act, ob_done, i, 2, b)
                    act.copy(oT[:], o_bank[:]).then_inc(oT_ready, 1)

            run(act, SCALAR_FIRST, SCALAR_ORDER, SCALAR_LAST, step)

        @block.vector
        def _(dve):
            def step(name, i, k, b, slot, turn):
                xt = xs[slot]
                first = isinstance(b, int) and b == 0
                if name == "W_LO":
                    dve.wait_ge(wl_hi_ready, 1)
                    dve.tensor_tensor(wl_lo[:], wl_raw, wl_hi[:].bitcast(F32),
                                      ALU.subtract).then_inc(wl_ready, 1)
                elif name == "WA_LO":
                    dve.wait_ge(wa_hi_ready, 1)
                    dve.tensor_tensor(wa_lo[:], wa_raw, wa_hi[:].bitcast(F32),
                                      ALU.subtract).then_inc(wa_ready, 1)
                elif name == "DEG":
                    dve.wait_ge(adj_loaded[i], 16)
                    dve.tensor_reduce(deg[:, i:i + 1], adj_raw[i], mybir.AxisListType.X,
                                      ALU.add).then_inc(deg_ready, 1)
                elif name == "MASK":
                    dve.wait_ge(deg_ready, i + 1)
                    dve.tensor_scalar(mask[:, i // 2, :], adj_raw[i], -NEG, NEG, ALU.mult,
                                      ALU.add).then_inc(mask_ready, 1)
                elif name == "DEG_MI":
                    dve.wait_ge(deg_ready, 2 * i + 2)
                    dve.wait_ge(l0_read, 2 * i + 2)
                    dve.wait_ge(xn_ready["1"], i // 2 + 1)
                    for t in (2 * i, 2 * i + 1):
                        ins = dve.scalar_tensor_tensor(xt[:, t, :], mi_bias[:, t, :], deg[:, t:t + 1], xt[:, t, :],
                                                       ALU.mult, ALU.add)
                    ins.then_inc(deg_mi_ready, 1)
                elif name in ("STATS1", "STATS2"):
                    n = name[-1]
                    which = int(n) - 1
                    if n == "1":
                        dve.wait_ge(x_loaded[slot][i], turn * 16 + 16)
                    else:
                        dve.wait_ge(x1_ready, b * 4 + (2 * i + 2))
                    after(dve, moments_ready[n], i + 1 - 2, 2, b)
                    for q in range(4):
                        ins = dve.bn_stats(stats[:, which, i, q, :], xt[:, 4 * i + q, :])
                    ins.then_inc(bn_done[n], 1)
                    dve.wait_ge(bn_done[n], b * 2 + (i + 1))
                    after(dve, xn_ready[n], i + 1 - 2, 2, b)
                    dve.sem_inc(dve_passed)
                    for q in range(4):
                        ins = dve.bn_aggr(moments[:, which, i, q, :], stats[:, which, i, q, :])
                    ins.then_inc(moments_ready[n], 1)
                elif name in ("LO1", "LO2"):
                    n = name[-1]
                    cols = slice(512 * i, 512 * i + 512)
                    dve.wait_ge(t_hi[n], b * 4 + (2 * i + k + 1))
                    dve.scalar_tensor_tensor(hT_lo[:, k, cols], bank_of("TRANSPOSE" + n, i, k)[:], 0.0,
                                             hT_hi[:, k, cols].bitcast(F32), ALU.max,
                                             ALU.subtract).then_inc(t_lo[n], 1)
                elif name == "MJ_LO_MI":
                    bank = bank_of("LINEAR", i)
                    dve.wait_ge(mjhi_ready, b * 8 + (i + 1))
                    dve.tensor_tensor(mj_lo[:, i, :], bank[:, D:2 * D], mj_hi[:, i, :].bitcast(F32), ALU.subtract)
                    if first:
                        if i == 0:
                            dve.wait_ge(small_loaded, 32)
                        dve.tensor_tensor(mi_bias[:, i, :], bank[:, 0:D], degb[:, 0, :], ALU.add).then_inc(l0_read, 1)
                        return
                    if i % 4 == 0:
                        dve.wait_ge(xb_ready, b * 2 + (i // 4 - 1))
                    dve.scalar_tensor_tensor(xt[:, i, :], bank[:, 0:D], deg[:, i:i + 1], xt[:, i, :], ALU.mult,
                                             ALU.add).then_inc(l0_read, 1)
                elif name == "X1":
                    rows = xt[:, 2 * i:2 * i + 2, :]
                    dve.wait_ge(done["AGGREGATE"], b * 4 + (i + 1))
                    if first:
                        dve.wait_ge(deg_mi_ready, i + 1)
                    dve.tensor_tensor(rows, bank_of("AGGREGATE", i)[:].rearrange("p (t d) -> p t d", t=2), rows,
                                      ALU.add).then_inc(x1_ready, 1)
                elif name == "S_ADD":
                    bank = bank_of("HH_BACK", i)
                    rows = xt[:, 4 * i:4 * i + 4, H:D]
                    dve.wait_ge(done["HH_BACK"], b * 2 + (i + 1))
                    if i == 0:
                        after(dve, relu_ready, 0, 8, b)
                    after(dve, s_ready, i, 2, b)
                    if first and i == 0:
                        dve.wait_ge(att_loaded, 32)
                    for q in range(4):
                        ins = dve.tensor_tensor_reduce(s_products[:, q, :], bank[:, H * q:H * q + H], a0_bc[:],
                                                       1.0 - SLOPE, 0.0, ALU.mult, ALU.add,
                                                       s_rest[:, 4 * i + q:4 * i + q + 1])
                    ins.then_inc(s_ready, 1)
                    dve.wait_ge(xn_ready["2"], b * 2 + (i + 1))
                    dve.tensor_tensor(rows, bank[:].rearrange("p (q h) -> p q h", q=4), rows,
                                      ALU.add).then_inc(xh_ready, 1)
                elif name == "HH_LO":
                    rows = (slice(None), slice(4 * i, 4 * i + 4))
                    dve.wait_ge(hhhi_ready, b * 2 + (i + 1))
                    dve.tensor_tensor(hh_lo[rows], bank_of("HH_BACK", i)[:].rearrange("p (q h) -> p q h", q=4),
                                      hh_hi[rows].bitcast(F32), ALU.subtract).then_inc(hh_ready, 1)
                elif name == "SCORES":
                    row = p_row[:, i % 2, :]
                    dve.wait_ge(relu_ready, b * 8 + (i + 1))
                    dve.wait_ge(nmask_ready, b * 8 + (i + 1))
                    if i == 0:
                        after(dve, p_ready, 0, 8, b)
                    dve.sem_inc(dve_passed)
                    dve.tensor_tensor_reduce(row, row, n_mask[:, i % 2, :], -1.0, FAR, ALU.add, ALU.min,
                                             neg_max[:, i:i + 1]).then_inc(e_ready, 1)
                elif name == "P_LO":
                    part = (slice(None), slice(4 * k, 4 * k + 4), slice(P * (i % 4), P * (i % 4) + P))
                    dve.wait_ge(phi_ready, b * 16 + (2 * i + k + 1))
                    dve.tensor_tensor(pT_lo[part], p_bank[(2 * i + k) % 4][:].rearrange("p (j i) -> p j i", j=4),
                                      pT_hi[part].bitcast(F32), ALU.subtract).then_inc(plo_ready, 1)
                else:
                    dve.wait_ge(p_ready, b * 8 + (4 * i + 4))
                    dve.reciprocal(rden[:, 4 * i:4 * i + 4], den[:, 4 * i:4 * i + 4]).then_inc(rden_ready, 1)
                    dve.wait_ge(rden_ready, b * 2 + (i + 1))
                    dve.wait_ge(ob_done, b * 2 + (i + 1))
                    for q in range(4):
                        t = 4 * i + q
                        ins = dve.scalar_tensor_tensor(xt[:, t, 0:H], o_bank[:, H * q:H * q + H], rden[:, t:t + 1],
                                                       xt[:, t, 0:H], ALU.mult, ALU.add)
                    ins.then_inc(out_ready, 1)

            run(dve, VECTOR_FIRST, VECTOR_ORDER, VECTOR_LAST, step)

        @block.tensor
        def _(pe):
            def free_bank(name, i, k, b):
                before, earlier = ring_before((name, i, k))
                per = PER_BATCH[before[0]]
                after(pe, ring_read[before[0]], ordinal(*before) - (per if earlier else 0), per, b)
                return bank_of(name, i, k)

            def products(bank, pairs):
                for n, (w, m) in enumerate(pairs):
                    ins = nc.tensor.matmul(bank, w, m, start=n == 0, stop=n == len(pairs) - 1)
                return ins

            def transposes(bank, tiles):
                for q, tile in enumerate(tiles):
                    ins = nc.tensor.transpose(bank[:, P * q:P * q + P], tile, ident[:])
                return ins

            def step(name, i, k, b, slot, turn):
                first = isinstance(b, int) and b == 0
                if name in ("TRANSPOSE1", "TRANSPOSE2"):
                    pe.wait_ge(xn_ready[name[-1]], b * 2 + (i + 1))
                    if first and name == "TRANSPOSE1" and i + k == 0:
                        pe.wait_ge(ident_loaded, 16)
                    bank = free_bank(name, i, k, b)
                    transposes(bank, [xn[:, i, q, P * k:P * k + P] for q in range(4)]).then_inc(done[name], 1)
                elif name == "LINEAR":
                    if i % 4 == 0:
                        pe.wait_ge(t_lo["1"], b * 4 + (2 * (i // 4) + 2))
                    if first and i == 0:
                        pe.wait_ge(wl_ready, 1)
                    bank = free_bank(name, i, 0, b)
                    rows = slice(P * i, P * i + P)
                    products(bank[:], [pair for f in range(K) for pair in (
                        (hT_hi[:, f, rows], wl_hi[:, f, :]), (hT_hi[:, f, rows], wl_lo[:, f, :]),
                        (hT_lo[:, f, rows], wl_hi[:, f, :]))]).then_inc(done[name], 1)
                elif name == "AGGREGATE":
                    if i + k == 0:
                        pe.wait_ge(l0_read, b * 8 + 8)
                        if first:
                            pe.wait_ge(adjt_ready, 8)
                    bank = bank_of(name, i) if k else free_bank(name, i, 0, b)
                    rows = slice(P * (2 * i + k), P * (2 * i + k) + P)
                    ins = products(bank[:, D * k:D * k + D], [
                        (adjT[:, j, rows], part[:, j, :]) for j in range(T) for part in (mj_hi, mj_lo)])
                    if k:
                        ins.then_inc(done[name], 1)
                elif name == "HH":
                    pe.wait_ge(t_lo["2"], b * 4 + (2 * i + 2))
                    if first and i == 0:
                        pe.wait_ge(wa_ready, 1)
                    bank = free_bank(name, i, 0, b)
                    cols = slice(512 * i, 512 * i + 512)
                    products(bank[:], [pair for f in range(K) for pair in (
                        (wa_hi[:, f, :], hT_hi[:, f, cols]), (wa_hi[:, f, :], hT_lo[:, f, cols]),
                        (wa_lo[:, f, :], hT_hi[:, f, cols]))]).then_inc(done[name], 1)
                elif name == "N_ROW":
                    pe.wait_ge(hht_ready, b * 2 + (i + 1))
                    if first and i == 0:
                        pe.wait_ge(att_loaded, 32)
                    bank = free_bank(name, i, 0, b)
                    products(bank[:], [(a1_col[:].broadcast_to([P, P]), hhT[:, i, :])]).then_inc(done[name], 1)
                elif name == "HH_BACK":
                    pe.wait_ge(hht_ready, b * 2 + (i + 1))
                    bank = free_bank(name, i, 0, b)
                    transposes(bank, [hhT[:, i, P * q:P * q + P] for q in range(4)]).then_inc(done[name], 1)
                elif name == "WARM":
                    pe.wait_ge(nb_ready, 2 * B)
                    for _ in range(5):
                        nc.tensor.matmul(bank_of("N_ROW", 1)[:], wl_hi[:, 0, 0:P], wl_hi[:, 0, :], start=True, stop=True)
                elif name == "P_BACK":
                    pe.wait_ge(p_ready, b * 8 + (i + 1))
                    after(pe, plo_ready, 2 * i + k - 3, 16, b)
                    transposes(p_bank[(2 * i + k) % 4],
                               [p_row[:, i % 2, P * j:P * j + P] for j in range(4 * k, 4 * k + 4)]).then_inc(tp_done, 1)
                elif name == "ATTEND":
                    if i + k == 0:
                        pe.wait_ge(hh_ready, b * 2 + 2)
                    if k == 0:
                        after(pe, out_ready, i, 2, b)
                    pe.wait_ge(plo_ready, b * 16 + (8 * i + 7 + k))
                    for j in range(4 * k, 4 * k + 4):
                        for n, (w, m) in enumerate(((hh_hi, pT_hi), (hh_hi, pT_lo), (hh_lo, pT_hi))):
                            ins = nc.tensor.matmul(o_bank[:], w[:, j, :], m[:, j, :], start=j + n == 0,
                                                   stop=j == T - 1 and n == 2)
                    ins.then_inc(att_done, 1)
                else:
                    pe.wait_ge(oT_ready, b * 2 + (i + 1))
                    transposes(o_bank, [oT[:, P * q:P * q + P] for q in range(4)]).then_inc(ob_done, 1)

            run(pe, TENSOR_FIRST, TENSOR_ORDER, TENSOR_LAST, step)


def kernel(x, adj, L0_gnn_W, L0_gnn_b, L1_gnn_W, L1_gnn_a):
    import numpy as np
    import concourse.bacc as bacc
    from concourse.bass_utils import run_bass_kernel_spmd

    t = adj.shape[0] // P
    tiled = np.asarray(adj).reshape(P, t, P, t)
    din = x.shape[-1]
    w = np.asarray(L0_gnn_W)
    arrays = {
        "x": np.asarray(x),
        "adj": tiled.transpose(0, 1, 3, 2).reshape(P, t, -1),
        "adj_t": tiled.transpose(2, 3, 1, 0).reshape(P, t, -1),
        "w_cat_t": np.concatenate([w[:, :din].T, w[:, din:].T], axis=1),
        "bias": np.asarray(L0_gnn_b),
        "w_att": np.asarray(L1_gnn_W),
        "a_self": np.asarray(L1_gnn_a)[0, :, 0],
        "a_neigh": np.asarray(L1_gnn_a)[1],
        "identity": np.eye(P, dtype=np.float32),
    }
    arrays = {f"in_{k}": np.ascontiguousarray(v) for k, v in arrays.items()}
    nc = bacc.Bacc("TRN2", target_bir_lowering=False, num_devices=1)
    args = [nc.dram_tensor(k, v.shape, mybir.dt.from_np(v.dtype), kind="ExternalInput").ap() for k, v in arrays.items()]
    out = nc.dram_tensor("out", x.shape, F32, kind="ExternalOutput").ap()
    build(nc, *args, out)
    result = run_bass_kernel_spmd(nc, [arrays], core_ids=[0])
    return result.results[0]["out"]
```
